# Optimizing a Trainium2 kernel written in Bass

```python
import numpy as np
import jax
import jax.numpy as jnp

def _softmax(x, axis=-1):
    return jax.nn.softmax(x, axis=axis)

def _gelu(x):
    return jax.nn.gelu(x, approximate=True)

def _silu(x):
    return jax.nn.silu(x)

def _sigmoid(x):
    return jax.nn.sigmoid(x)

def _layernorm(x, axis=-1, eps=1e-05):
    m = jnp.mean(x, axis=axis, keepdims=True)
    v = jnp.var(x, axis=axis, keepdims=True)
    return (x - m) / jnp.sqrt(v + eps)

def _scatter_add(tgt, idx, src, axis=0):
    return tgt.at[idx].add(src)

def _segment_sum(src, seg, n):
    return jax.ops.segment_sum(src, seg, n)
kernel_name = 'mk_gnn_resnorm_d2_gnn_r8_9b8ecd'

def setup_inputs(seed: int=0):
    np.random.seed(seed)
    _w = jnp.asarray

    def _rec_inputs():
        import jax
        import jax.numpy as jnp
        _gk = jax.random.key(seed)
        x = -0.000202 + 1 * jax.random.normal(jax.random.fold_in(_gk, 1), (6250, 128), jnp.float32)
        _s = jax.random.randint(jax.random.fold_in(_gk, 2), (50000,), 0, 6250, jnp.int32)
        _d = jax.random.randint(jax.random.fold_in(_gk, 3), (50000,), 0, 6250, jnp.int32)
        _loop = jnp.arange(6250, dtype=jnp.int32)
        src = jnp.concatenate([_s, _d, _loop])
        dst = jnp.concatenate([_d, _s, _loop])
        _o = jnp.argsort(dst, stable=True)
        src = src[_o]
        dst = dst[_o]
        edge_attr_128 = -4.21973e-05 + 0.999841 * jax.random.normal(jax.random.fold_in(_gk, 12), (106250, 128), jnp.float32)
        return (x, src, dst, edge_attr_128)
    x, src, dst, edge_attr_128 = _rec_inputs()

    def _L0_gnn_setup():
        import jax, jax.numpy as jnp
        import numpy as np
        N_NODES = 6250
        N_EDGES = 200000
        IN_DIM = 128
        OUT_DIM = 128
        NEG_SLOPE = 0.01
        key = jax.random.key(seed)
        ks = jax.random.split(key, 8)
        feat = jax.random.normal(ks[0], (N_NODES, IN_DIM), dtype=jnp.float32)
        src = jax.random.randint(ks[1], (N_EDGES,), 0, N_NODES, dtype=jnp.int32)
        dst = jax.random.randint(ks[2], (N_EDGES,), 0, N_NODES, dtype=jnp.int32)
        W = jax.random.normal(ks[3], (IN_DIM, OUT_DIM), dtype=jnp.float32) / np.sqrt(IN_DIM)
        b = jax.random.normal(ks[4], (OUT_DIM,), dtype=jnp.float32) * 0.01
        attn_w = jax.random.normal(ks[5], (2 * OUT_DIM, 1), dtype=jnp.float32) / np.sqrt(2 * OUT_DIM)
        attn_b = jax.random.normal(ks[6], (1,), dtype=jnp.float32) * 0.01
        mask_weights = jnp.ones((IN_DIM,), dtype=jnp.float32)
        return {'feat': feat, 'src': src, 'dst': dst, 'W': W, 'b': b, 'attn_w': attn_w, 'attn_b': attn_b, 'mask_weights': mask_weights}
    _L0_gnn_all = _L0_gnn_setup()
    _L0_gnn_in = {k: v for k, v in _L0_gnn_all.items() if k in ('W', 'b', 'attn_w', 'attn_b', 'mask_weights')}
    del _L0_gnn_all

    def _L1_gnn_setup():
        import jax, jax.numpy as jnp
        import numpy as np
        N_NODES = 6250
        N_EDGES = 75000
        D = 128
        D_OUT = 128
        key = jax.random.key(seed)
        k1, k2, k3, k4, k5, k6 = jax.random.split(key, 6)
        node_feats = jax.random.normal(k1, (N_NODES, D), dtype=jnp.float32)
        edge_feats = jax.random.normal(k2, (N_EDGES, D), dtype=jnp.float32)
        src = jax.random.randint(k3, (N_EDGES,), 0, N_NODES)
        dst = jax.random.randint(k4, (N_EDGES,), 0, N_NODES)
        W = jax.random.normal(k5, (D_OUT, 2 * D), dtype=jnp.float32) * (1.0 / np.sqrt(2 * D))
        b = jax.random.normal(k6, (D_OUT,), dtype=jnp.float32) * 0.01
        return {'node_feats': node_feats, 'edge_feats': edge_feats, 'src': src, 'dst': dst, 'W': W, 'b': b}
    _L1_gnn_all = _L1_gnn_setup()
    _L1_gnn_in = {k: v for k, v in _L1_gnn_all.items() if k in ('W', 'b')}
    del _L1_gnn_all
    return {'x': x, 'src': src, 'dst': dst, 'edge_attr_128': edge_attr_128, 'L0_gnn_W': _L0_gnn_in['W'], 'L0_gnn_b': _L0_gnn_in['b'], 'L0_gnn_attn_w': _L0_gnn_in['attn_w'], 'L0_gnn_attn_b': _L0_gnn_in['attn_b'], 'L0_gnn_mask_weights': _L0_gnn_in['mask_weights'], 'L1_gnn_W': _L1_gnn_in['W'], 'L1_gnn_b': _L1_gnn_in['b']}

def reference(x, src, dst, edge_attr_128, L0_gnn_W, L0_gnn_b, L0_gnn_attn_w, L0_gnn_attn_b, L0_gnn_mask_weights, L1_gnn_W, L1_gnn_b):
    import jax
    import jax.numpy as jnp

    def _L0_gnn_ref(feat, src, dst, W, b, attn_w, attn_b, mask_weights):
        import jax, jax.numpy as jnp
        import numpy as np
        N_NODES = 6250
        N_EDGES = 200000
        IN_DIM = 128
        OUT_DIM = 128
        NEG_SLOPE = 0.01
        N = feat.shape[0]
        d = W.shape[1]
        h = feat * jax.nn.sigmoid(mask_weights) @ W + b
        s_src = (h @ attn_w[:d]).squeeze(-1)
        s_dst = (h @ attn_w[d:]).squeeze(-1)
        score = s_src[src] + s_dst[dst] + attn_b[0]
        score = jnp.where(score >= 0, score, NEG_SLOPE * score)
        mx = jax.ops.segment_max(score, dst, num_segments=N)
        mx = jnp.where(jnp.isfinite(mx), mx, 0.0)
        ex = jnp.exp(score - mx[dst])
        denom = jax.ops.segment_sum(ex, dst, num_segments=N)
        a = ex / jnp.where(denom == 0, 1.0, denom)[dst]
        h_new = jax.ops.segment_sum(h[src] * a[:, None], dst, num_segments=N)
        return h_new

    def _L1_gnn_ref(node_feats, edge_feats, src, dst, W, b):
        import jax, jax.numpy as jnp
        import numpy as np
        N_NODES = 6250
        N_EDGES = 75000
        D = 128
        D_OUT = 128
        n = node_feats.shape[0]
        msg = node_feats[src] + edge_feats
        neigh_sum = jax.ops.segment_sum(msg, dst, num_segments=n)
        deg = jax.ops.segment_sum(jnp.ones((msg.shape[0],), dtype=node_feats.dtype), dst, num_segments=n)
        neigh = neigh_sum / jnp.clip(deg, 1.0)[:, None]
        combined = jnp.concatenate([neigh, node_feats], axis=1)
        return combined @ W.T + b
    x = _layernorm(x + _L0_gnn_ref(x, src, dst, L0_gnn_W, L0_gnn_b, L0_gnn_attn_w, L0_gnn_attn_b, L0_gnn_mask_weights), axis=-1)
    x = _layernorm(x + _L1_gnn_ref(x, edge_attr_128, src, dst, L1_gnn_W, L1_gnn_b), axis=-1)
    return x

_drawn_inputs = setup_inputs


def setup_inputs(seed=0):
    import zlib

    import numpy as np

    out = dict(_drawn_inputs(seed))
    spreads = {'L0_gnn_mask_weights': (1.0, 0.6)}
    factors = {'L0_gnn_b': 4.513, 'L1_gnn_b': 6.002}
    for name, (base, spread) in spreads.items():
        noise = np.random.default_rng([zlib.crc32(name.encode()), seed]).standard_normal(out[name].shape)
        drawn = base * np.exp(spread * noise) if base else spread * noise
        out[name] = jnp.asarray(drawn.astype(out[name].dtype))
    for name, factor in factors.items():
        out[name] = (out[name] * factor).astype(out[name].dtype)
    return out
```

```python
import concourse.bass as bass
from concourse import mybir
from contextlib import ExitStack

N = 6250
E = 106250
D = 128
P = 128
LEAK = 0.01
EPS = 1e-5

K = 4
GE = K * P
NG = -(-E // GE)
HOLE = NG * GE - E
U = 8
NB = NG // U
WIN = 40
MAXP = -(-N // WIN)
T = -(-N // P)
LAST = N - (T - 1) * P
Q = 4
COLS = N + WIN
NBATCH = (T - 1) // Q
MASKED = -1.0e30
FLOOR = -1.0e25
TINY = 1.0e-30
assert NG % U == 0 and NBATCH % 2 == 0 and (T - 1) % Q == 0 and HOLE < GE


def gnn_program(nc, x, src, dst, edge, w0, b0, aw, ab, mask, w1, b1, out):
    fp32 = mybir.dt.float32
    i32 = mybir.dt.int32
    ALU = mybir.AluOpType
    ACT = mybir.ActivationFunctionType
    AX = mybir.AxisListType.X

    ctx = ExitStack()
    with ctx:
        def sb(name, shape, dt=fp32):
            return ctx.enter_context(nc.sbuf_tensor(name, shape, dt))

        def sem(name):
            return ctx.enter_context(nc.semaphore(name))

        htab = nc.dram_tensor("htab", [N, D + 1], fp32).ap()
        x1tab = nc.dram_tensor("x1tab", [N, D], fp32).ap()
        srcp = nc.dram_tensor("srcp", [NG * GE], i32).ap()
        dstp = nc.dram_tensor("dstp", [NG * GE], i32).ap()

        ident = sb("ident", [P, P])
        ones = sb("ones", [P, P])
        iota_i = sb("iota_i", [P, WIN], i32)
        iota_w = sb("iota_w", [P, WIN])
        steps_i = sb("steps_i", [P, MAXP], i32)
        steps = sb("steps", [P, MAXP])
        fill_i = sb("fill_i", [1, 2, HOLE], i32)
        w0_sb = sb("w0_sb", [P, D])
        wext = sb("wext", [P, D + 1])
        a_b = sb("a_b", [P, 2, D])
        b0_b = sb("b0_b", [P, D])
        ab_b = sb("ab_b", [P, 1])
        mask_sb = sb("mask_sb", [P, 1])
        sig = sb("sig", [P, 3])
        prod = sb("prod", [P, 4, D])
        dots = sb("dots", [P, 4])
        wdst = sb("wdst", [P, P])
        w1_sb = sb("w1_sb", [P, 2 * D])
        wa_t = sb("wa_t", [P, D])
        wb_t = sb("wb_t", [P, D])
        b1_row = sb("b1_row", [1, D])
        eps_c = sb("eps_c", [P, 1])
        sdb_c = sb("sdb_c", [P, 1])

        rng = sb("rng", [P, 2, GE], i32)
        ext = sb("ext", [P, 2, 2])
        lohi = sb("lohi", [P, 2, NG])
        span = sb("span", [P, NG])
        span_max = sb("span_max", [P, 1])
        reach = sb("reach", [P, MAXP])
        passes = sb("passes", [P, 1])
        passes_i = sb("passes_i", [P, 1], i32)
        base_f = sb("base_f", [P, NG])
        base_i = sb("base_i", [P, NG], i32)

        x_sb = sb("x_sb", [P, T, D])
        x_t = sb("x_t", [P, 2, Q * P])
        h_sb = sb("h_sb", [P, 2, Q, D + 1])
        y_sb = sb("y_sb", [P, 2, Q, D])
        o_sb = sb("o_sb", [P, 2, Q, D])
        stats = sb("stats", [P, 2, Q, 6])
        mv = sb("mv", [P, 2, Q, 2])
        std = sb("std", [P, 2, Q])
        rstd = sb("rstd", [P, 2, Q])
        shift = sb("shift", [P, 2, Q])
        inv = sb("inv", [P, 2, Q * P])
        norm = sb("norm", [P, 2, Q * P])
        md = sb("md", [P, 2, COLS])
        agg = sb("agg", [P, 2, COLS])

        src_i = sb("src_i", [P, U, K], i32)
        dst_i = sb("dst_i", [P, U, K], i32)
        dst_f = sb("dst_f", [P, U, K])
        rel = sb("rel", [P, U, K])
        rows = sb("rows", [P, U, K, D + 1])
        ef = sb("ef", [P, U, K, D])
        hot = sb("hot", [P, 2, K, WIN])
        comb = sb("comb", [P, 2, K, WIN])
        zed = sb("zed", [P, 2, K, WIN])
        lrel = sb("lrel", [P, 2, K + 1, WIN])
        prob = sb("prob", [P, 2, K + 1, WIN])
        top = sb("top", [WIN, 2])

        bank = [ctx.enter_context(nc.psum_tensor(f"bank{i}", [P, 512], fp32)) for i in range(8)]

        def sems(name, n):
            return [sem(f"{name}{i}") for i in range(n)]

        s_const = sem("s_const")
        s_zero = sem("s_zero")
        s_fill = sem("s_fill")
        s_wload = sem("s_wload")
        s_xload = sem("s_xload")
        s_x = sems("s_x", 2)
        s_rng = sem("s_rng")
        s_padded = sem("s_padded")
        s_prep = sem("s_prep")
        s_gate = sem("s_gate")
        s_ext = sem("s_ext")
        s_lohi = sem("s_lohi")
        s_bases = sem("s_bases")
        s_weights = sem("s_weights")
        s_w1t = sem("s_w1t")
        s_w1c = sem("s_w1c")
        s_xt = sems("s_xt", 2)
        s_xtc = sems("s_xtc", 2)
        s_h = sems("s_h", 2)
        s_hs = sems("s_hs", 2)
        s_sd = sems("s_sd", 2)
        s_htab = sems("s_htab", 2)
        s_clear = sem("s_clear")
        s_ot = sems("s_ot", 2)
        s_otc = sems("s_otc", 2)
        s_own = sems("s_own", 2)
        s_owned = sems("s_owned", 2)

        idx = [sems("s0_idx", 2), sems("s1_idx", 2)]
        gath = [sems("s0_gath", U), sems("s1_gath", U)]
        s_ef = sems("s_ef", U)
        s_msg = sems("s_msg", U)
        dstf = [sem("s0_dstf"), sem("s1_dstf")]
        relw = [sem("s0_rel"), sem("s1_rel")]
        hotw = [sem("s0_hot"), sem("s1_hot")]
        s_comb = sem("s_comb")
        s_zed = sem("s_zed")
        s_leak = sem("s_leak")
        s_turn = sem("s_turn")
        s_top = sem("s_top")
        s_max = sem("s_max")
        s_old = sem("s_old")
        s_new = sem("s_new")
        s_arg = sem("s_arg")
        s_prob = sem("s_prob")
        sums = [sems("s0_sum", U), sems("s1_sum", U)]
        s_scaled = sem("s_scaled")
        acc = [sem("s0_acc"), sem("s1_acc")]
        moved = [sem("s0_moved"), sem("s1_moved")]

        class Finish:
            def __init__(self, l):
                self.mean = sems(f"{l}_mean", 2)
                self.mm = sems(f"{l}_mm", 2)
                self.y = sems(f"{l}_y", 2)
                self.stats = sems(f"{l}_stats", 2)
                self.mv = sems(f"{l}_mv", 2)
                self.std = sems(f"{l}_std", 2)
                self.rstd = sems(f"{l}_rstd", 2)
                self.shift = sems(f"{l}_shift", 2)
                self.normed = sems(f"{l}_normed", 2)
                self.store = sems(f"{l}_store", 2)
                self.all_stored = [16 * (NBATCH // 2 + 1), 16 * (NBATCH // 2)]

        F0, F1 = Finish("f0"), Finish("f1")
        s_held = sem("s_held")

        def hold(eng, sem, value):
            eng.wait_ge(sem, value)
            eng.sem_inc(s_held, 1)

        block = ctx.enter_context(nc.Block())

        def per_batch(eng, body):
            with eng.Fori(0, NBATCH // 2) as i:
                for j in range(2):
                    body(i, j, (i * 2 + j) * Q, Q, P)
            body(NBATCH // 2, 0, T - 1, 1, LAST)

        def tile_rows(dram, t, n, r):
            if n == 1:
                return dram[t * P:t * P + r, :]
            return dram[bass.ds(t * P, n * P), :].rearrange("(t p) d -> p t d", p=P)

        def tiles(buf, t, n, r):
            return buf[0:r, t, :] if n == 1 else buf[:, bass.ds(t, n), :]

        def cols(t, n, r):
            return slice(t * P, t * P + r) if n == 1 else bass.ds(t * P, n * P)

        def split(ap):
            return ap.rearrange("p (t d) -> p t d", d=D)

        @block.sync
        def _(sp):
            half = NG - P
            sp.dma_start(rng[:, 0, :], dst[0:P * GE].rearrange("(g e) -> g e", g=P)).then_inc(s_rng, 16)
            sp.dma_start(rng[0:half - 1, 1, :], dst[P * GE:(NG - 1) * GE].rearrange("(g e) -> g e", g=half - 1)).then_inc(s_rng, 16)
            sp.dma_start(rng[half - 1:half, 1, :], dst[E - GE:E].rearrange("(g e) -> g e", g=1)).then_inc(s_rng, 16)
            for into, what in ((mask_sb[:, :], mask.rearrange("(p a) -> p a", a=1)),
                               (w0_sb[:, :], w0), (w1_sb[:, :], w1),
                               (a_b[:, 0, :], aw[0:D, :].rearrange("d a -> a d").to_broadcast([P, D])),
                               (a_b[:, 1, :], aw[D:2 * D, :].rearrange("d a -> a d").to_broadcast([P, D])),
                               (b0_b[:, :], b0.rearrange("(a d) -> a d", a=1).to_broadcast([P, D])),
                               (ab_b[:, :], ab.rearrange("(a d) -> a d", a=1).to_broadcast([P, 1])),
                               (b1_row[:, :], b1.rearrange("(a d) -> a d", a=1))):
                sp.dma_start(into, what).then_inc(s_wload, 16)
            full = (NG - 1) * GE
            sp.wait_ge(s_fill, 2)
            for m, (lst, pad) in enumerate(((src, srcp), (dst, dstp))):
                sp.dma_start(pad[0:full].rearrange("(a b) -> a b", b=GE), lst[0:full].rearrange("(a b) -> a b", b=GE)).then_inc(s_padded, 16)
                sp.dma_start(pad[full:full + HOLE].rearrange("(a b) -> a b", a=1), fill_i[:, m, :]).then_inc(s_padded, 16)
                sp.dma_start(pad[full + HOLE:NG * GE].rearrange("(a b) -> a b", a=1), lst[full:E].rearrange("(a b) -> a b", a=1)).then_inc(s_padded, 16)
            sp.wait_ge(s_padded, 96)

            def store_h(i, j, t, n, r):
                sp.wait_ge(s_hs[j], 2 * i + 2)
                sp.dma_start(tile_rows(htab, t, n, r), h_sb[0:r, j, 0, :] if n == 1 else h_sb[:, j, :, :]).then_inc(s_htab[j], 16)
            per_batch(sp, store_h)
            sp.dma_start(x_sb[:, 0:T - 1, :], x[0:(T - 1) * P, :].rearrange("(t p) d -> p t d", p=P)).then_inc(s_xload, 16)
            sp.dma_start(x_sb[0:LAST, T - 1, :], x[(T - 1) * P:N, :]).then_inc(s_xload, 16)

            sp.wait_ge(s_bases, 1)
            npass = sp.value_load(passes_i[0:1, 0:1], min_val=1, max_val=MAXP)

            def load_body(l, v, it, last):
                H = U // 2
                for h in range(2):
                    sp.wait_ge(dstf[l], v)
                    for u in range(h * H, (h + 1) * H):
                        sp.wait_ge(gath[l][u], v * K * 16)
                    for buf, lst in ((src_i, srcp), (dst_i, dstp)):
                        sp.dma_start(buf[:, h * H:(h + 1) * H, :],
                                     lst[bass.ds((it * U + h * H) * GE, H * GE)].rearrange("(g p k) -> p g k", p=P, k=K)).then_inc(idx[l][h], 16)
                    for u in range(h * H, (h + 1) * H) if l else ():
                        e0 = E - GE if last and u == U - 1 else (it * U + u) * GE
                        sp.wait_ge(s_msg[u], v)
                        sp.dma_start(ef[:, u, :, :], edge[bass.ds(e0, GE), :].rearrange("(p k) d -> p k d", k=K)).then_inc(s_ef[u], 16)

            def load_edges(l):
                with sp.Fori(0, npass) as w:
                    with sp.Fori(0, NB - 1) as it:
                        load_body(l, w * NB + it, it, False)
                    load_body(l, w * NB + NB - 1, NB - 1, True)

            load_edges(0)

            def store_x1(i, j, t, n, r):
                sp.wait_ge(F0.normed[j], i + 1)
                sp.dma_start(tile_rows(x1tab, t, n, r), o_sb[0:r, j, 0, :] if n == 1 else o_sb[:, j, :, :]).then_inc(F0.store[j], 16)
            per_batch(sp, store_x1)
            load_edges(1)

            def store_out(i, j, t, n, r):
                sp.wait_ge(F1.normed[j], i + 1)
                sp.dma_start(tile_rows(out, t, n, r), o_sb[0:r, j, 0, :] if n == 1 else o_sb[:, j, :, :]).then_inc(F1.store[j], 16)
            per_batch(sp, store_out)
            for j in range(2):
                sp.wait_ge(F1.store[j], F1.all_stored[j])

        @block.gpsimd
        def _(pool):
            pool.memset(fill_i[:, 0, :], 0).then_inc(s_fill, 1)
            pool.memset(fill_i[:, 1, :], -1).then_inc(s_fill, 1)
            pool.memset(ident[:, :], 0.0).then_inc(s_zero, 1)
            pool.wait_ge(s_zero, 1)
            pool.affine_select(out=ident[:, :], in_=ident[:, :], compare_op=ALU.not_equal, fill=1.0, base=0,
                               pattern=[[-1, P]], channel_multiplier=1).then_inc(s_const, 1)
            pool.memset(ones[:, :], 1.0).then_inc(s_const, 1)
            pool.iota(iota_i[:, :], pattern=[[1, WIN]], base=0, channel_multiplier=0).then_inc(s_const, 1)
            pool.iota(steps_i[:, :], pattern=[[WIN, MAXP]], base=0, channel_multiplier=0).then_inc(s_const, 1)
            pool.memset(eps_c[:, :], EPS).then_inc(s_const, 1)
            pool.memset(md[:, 1, N:COLS], 0.0).then_inc(s_const, 1)
            pool.memset(md[:, 0, :], FLOOR).then_inc(s_const, 1)
            pool.memset(agg[:, :, :], 0.0).then_inc(s_const, 1)
            def load_x(i, j, t, n, r):
                pool.wait_ge(s_xt[j], i)
                pool.dma_start(y_sb[0:r, j, 0, :] if n == 1 else y_sb[:, j, :, :], tile_rows(x, t, n, r)).then_inc(s_x[j], 16)
            per_batch(pool, load_x)
            pool.wait_ge(s_bases, 1)
            npass = pool.value_load(passes_i[0:1, 0:1], min_val=1, max_val=MAXP)

            def gather_rows(l, table, width):
                with pool.Fori(0, npass) as w:
                    with pool.Fori(0, NB) as it:
                        v = w * NB + it
                        for u in range(U):
                            if u % (U // 2) == 0:
                                pool.wait_ge(idx[l][u // (U // 2)], v * 32 + 32)
                            hold(pool, sums[l][u], v)
                            for k in range(K):
                                pool.indirect_dma_start(
                                    rows[:, u, k, 0:width], None, table[:, :],
                                    bass.IndirectOffsetOnAxis(src_i[:, u, k:k + 1], 0)).then_inc(gath[l][u], 16)

            for j in range(2):
                pool.wait_ge(s_htab[j], F0.all_stored[j])
            gather_rows(0, htab, D + 1)
            pool.wait_ge(F0.mean[0], 1)
            pool.memset(md[:, :, :], 0.0).then_inc(s_clear, 1)
            for j in range(2):
                pool.wait_ge(F0.store[j], F0.all_stored[j])
            gather_rows(1, x1tab, D)

        @block.tensor
        def _(pe):
            pe.wait_ge(s_const, 2)
            pe.wait_ge(s_ext, 4)
            for m in range(2):
                for c, n in ((0, P), (1, NG - P)):
                    last = pe.matmul(bank[7][:, m * NG + c * P:m * NG + c * P + n],
                                     ext[0:n, c, m:m + 1].to_broadcast([n, P]), ident[0:n, 0:n], start=True, stop=True)
            last.then_inc(s_lohi, 1)
            pe.wait_ge(s_wload, 128)
            for m in range(2):
                last = pe.transpose(bank[5 + m][:, 0:D], w1_sb[:, m * D:(m + 1) * D], ident[:, :])
            last.then_inc(s_w1t, 1)
            pe.wait_ge(s_weights, 2)
            pe.wait_ge(s_w1c, 2)

            def node_scores(i, j, t, n, r):
                c = (n - 1) * P + r
                pe.wait_ge(s_x[j], 16 * i + 16)
                pe.wait_ge(s_xtc[j], i)
                for m in range(n):
                    last = pe.transpose(bank[j][:, m * P:m * P + r], y_sb[0:r, j, m, :], ident[0:r, 0:r])
                last.then_inc(s_xt[j], 1)
                pe.wait_ge(s_xtc[j], i + 1)
                pe.wait_ge(s_hs[j], 2 * i)
                pe.wait_ge(s_sd[j], i)
                for m in range(n):
                    pe.matmul(bank[2 + j][0:r, m * D:(m + 1) * D], x_t[:, j, m * P:m * P + r], wext[:, 0:D], start=True, stop=True)
                    pe.matmul(bank[6 + j][0:r, m:m + 1], x_t[:, j, m * P:m * P + r], wext[:, D:D + 1], start=True, stop=True)
                pe.matmul(bank[4 + j][:, 0:c], wdst[:, :], x_t[:, j, 0:c], start=True, stop=True).then_inc(s_h[j], 1)
            per_batch(pe, node_scores)

            npass = pe.value_load(passes_i[0:1, 0:1], min_val=1, max_val=MAXP)
            for j in range(2):
                pe.wait_ge(s_hs[j], 2 * (NBATCH // 2 + 1 - j))
                pe.wait_ge(s_sd[j], NBATCH // 2 + 1 - j)

            def group_sums(l, u):
                for k in range(K):
                    pe.matmul(bank[4 + u % 2][:, 0:WIN], rows[:, u, k, 0:D], prob[:, u % 2, k, :],
                              start=(k == 0), stop=(k == K - 1))
                for k in range(K):
                    last = pe.matmul(bank[4 + u % 2][:, WIN:2 * WIN], ones[:, :], prob[:, u % 2, k, :],
                                     start=(k == 0), stop=(k == K - 1))
                last.then_inc(sums[l][u], 1)

            with pe.Fori(0, npass) as w:
                with pe.Fori(0, NB) as it:
                    n0 = w * NG + it * U
                    for u in range(U + 1):
                        if u >= 1:
                            pe.wait_ge(s_top, n0 + u)
                            pe.matmul(bank[2 + (u - 1) % 2][:, 0:WIN], top[:, (u - 1) % 2:(u - 1) % 2 + 1].to_broadcast([WIN, P]),
                                      ident[0:WIN, 0:WIN], start=True, stop=True).then_inc(s_max, 1)
                        if u < U:
                            hold(pe, s_leak, n0 + u + 1)
                            for k in range(K):
                                last = pe.transpose(bank[u % 2][0:WIN, k * P:(k + 1) * P], lrel[:, u % 2, k, :], ident[:, :])
                            last.then_inc(s_turn, 1)
                        if u >= 1:
                            pe.wait_ge(s_prob, n0 + u)
                            group_sums(0, u - 1)

            def turn_back(i, j, t, n, r):
                pe.wait_ge(F0.mean[j], i + 1)
                pe.wait_ge(F0.y[j], i)
                for m in range(n):
                    last = pe.transpose(bank[j][0:r, m * D:(m + 1) * D], norm[:, j, m * P:m * P + r], ident[:, :])
                last.then_inc(F0.mm[j], 1)

            def own_part(i, j, t, n, r):
                pe.wait_ge(F0.normed[j], i + 1)
                pe.wait_ge(s_otc[j], i)
                for m in range(n):
                    last = pe.transpose(bank[2 + j][:, m * P:m * P + r], o_sb[0:r, j, m, :], ident[0:r, 0:r])
                last.then_inc(s_ot[j], 1)
                pe.wait_ge(s_otc[j], i + 1)
                pe.wait_ge(s_owned[j], i)
                for m in range(n):
                    pe.matmul(bank[6 + j][0:r, m * D:(m + 1) * D], x_t[:, j, m * P:m * P + r], wb_t[:, :], start=True, stop=False)
                    last = pe.matmul(bank[6 + j][0:r, m * D:(m + 1) * D], ones[0:1, 0:r], b1_row[:, :], start=False, stop=True)
                last.then_inc(s_own[j], 1)

            def end_first(i, j, t, n, r):
                turn_back(i, j, t, n, r)
                own_part(i, j, t, n, r)
            per_batch(pe, end_first)

            with pe.Fori(0, npass) as w:
                with pe.Fori(0, NB) as it:
                    v = w * NB + it
                    for u in range(U):
                        pe.wait_ge(s_msg[u], v + 1)
                        group_sums(1, u)

            def neighbours(i, j, t, n, r):
                pe.wait_ge(F1.mean[j], i + 1)
                pe.wait_ge(F1.y[j], i)
                for m in range(n):
                    last = pe.matmul(bank[j][0:r, m * D:(m + 1) * D], norm[:, j, m * P:m * P + r], wa_t[:, :], start=True, stop=True)
                last.then_inc(F1.mm[j], 1)
            per_batch(pe, neighbours)

        @block.scalar
        def _(act):
            act.wait_ge(s_wload, 128)
            act.activation(sig[:, 0:1], mask_sb[:, :], ACT.Exp, scale=-1.0).then_inc(s_gate, 1)
            act.wait_ge(s_w1t, 1)
            act.activation(wa_t[:, :], bank[5][:, 0:D], ACT.Copy).then_inc(s_w1c, 1)
            act.wait_ge(s_weights, 2)

            def scores_out(i, j, t, n, r):
                c = (n - 1) * P + r
                act.wait_ge(s_xt[j], i + 1)
                act.wait_ge(s_h[j], i)
                act.activation(x_t[:, j, 0:c], bank[j][:, 0:c], ACT.Copy).then_inc(s_xtc[j], 1)
                act.wait_ge(s_h[j], i + 1)
                act.activation(md[:, 1, cols(t, n, r)], bank[4 + j][:, 0:c], ACT.Identity, bias=sdb_c[:, :]).then_inc(s_sd[j], 1)
            per_batch(act, scores_out)

            npass = act.value_load(passes_i[0:1, 0:1], min_val=1, max_val=MAXP)
            with act.Fori(0, npass) as w:
                with act.Fori(0, NB) as it:
                    for u in range(U):
                        act.wait_ge(s_arg, w * NG + it * U + u + 1)
                        act.activation(prob[:, u % 2, :, :], lrel[:, u % 2, :, :], ACT.Exp).then_inc(s_prob, 1)

            def norm_rows(F, i, j, n, r):
                act.wait_ge(F.mv[j], i + 1)
                act.activation(std[0:r, j, 0:n], mv[0:r, j, 0:n, 1], ACT.Sqrt, bias=eps_c[0:r, :]).then_inc(F.std[j], 1)
                act.wait_ge(F.shift[j], i + 1)
                for m in range(n):
                    last = act.activation(o_sb[0:r, j, m, :], y_sb[0:r, j, m, :], ACT.Identity,
                                          bias=shift[0:r, j, m:m + 1], scale=rstd[0:r, j, m:m + 1])
                last.then_inc(F.normed[j], 1)

            def norm_x1(i, j, t, n, r):
                act.wait_ge(F0.store[j], 16 * i)
                act.wait_ge(s_ot[j], i)
                norm_rows(F0, i, j, n, r)

            def own_out(i, j, t, n, r):
                c = (n - 1) * P + r
                act.wait_ge(s_ot[j], i + 1)
                act.wait_ge(s_own[j], i)
                act.activation(x_t[:, j, 0:c], bank[2 + j][:, 0:c], ACT.Copy).then_inc(s_otc[j], 1)
                act.wait_ge(s_own[j], i + 1)
                act.wait_ge(F0.y[j], i + 1)
                act.activation(tiles(x_sb, t, n, r), bank[6 + j][0:r, 0:D] if n == 1 else split(bank[6 + j][:, :]), ACT.Copy).then_inc(s_owned[j], 1)

            def end_first(i, j, t, n, r):
                norm_x1(i, j, t, n, r)
                own_out(i, j, t, n, r)
            per_batch(act, end_first)

            def norm_out(i, j, t, n, r):
                act.wait_ge(F1.store[j], 16 * i)
                norm_rows(F1, i, j, n, r)
            per_batch(act, norm_out)

        @block.vector
        def _(dve):
            step = [0]

            def then(ins):
                step[0] += 1
                ins.then_inc(s_prep, 1)
                dve.wait_ge(s_prep, step[0])

            dve.wait_ge(s_rng, 48)
            for c, n in ((0, P), (1, NG - P)):
                dve.tensor_reduce(ext[0:n, c, 0:1], rng[0:n, c, :], AX, ALU.min).then_inc(s_ext, 1)
                dve.tensor_reduce(ext[0:n, c, 1:2], rng[0:n, c, :], AX, ALU.max).then_inc(s_ext, 1)
            dve.wait_ge(s_const, 4)
            then(dve.tensor_copy(iota_w[:, :], iota_i[:, :]))
            then(dve.tensor_copy(steps[:, :], steps_i[:, :]))
            dve.wait_ge(s_lohi, 1)
            then(dve.tensor_copy(lohi[:, :, :], bank[7][:, 0:2 * NG].rearrange("p (m g) -> p m g", m=2)))
            then(dve.tensor_tensor(span[:, :], lohi[:, 1, :], lohi[:, 0, :], ALU.subtract))
            then(dve.reduce_max(span_max[:, :], span[:, :], AX))
            then(dve.tensor_scalar(reach[:, :], steps[:, :], span_max[:, 0:1], None, ALU.is_le))
            then(dve.tensor_reduce(passes[:, :], reach[:, :], AX, ALU.add))
            then(dve.tensor_copy(passes_i[:, :], passes[:, :]))
            then(dve.tensor_copy(base_f[:, :], lohi[:, 0, :]))
            dve.tensor_copy(base_i[:, :], lohi[:, 0, :]).then_inc(s_bases, 1)
            dve.wait_ge(s_wload, 128)
            dve.wait_ge(s_gate, 1)
            then(dve.tensor_scalar_add(sig[:, 1:2], sig[:, 0:1], 1.0))
            then(dve.reciprocal(sig[:, 2:3], sig[:, 1:2]))
            then(dve.tensor_scalar(wext[:, 0:D], w0_sb[:, :], sig[:, 2:3], None, ALU.mult))
            for i in range(2):
                then(dve.tensor_tensor(prod[:, i, :], wext[:, 0:D], a_b[:, i, :], ALU.mult))
                then(dve.tensor_tensor(prod[:, 2 + i, :], b0_b[:, :], a_b[:, i, :], ALU.mult))
            then(dve.tensor_reduce(dots[:, :], prod[:, :, :], AX, ALU.add))
            then(dve.tensor_tensor(sdb_c[:, :], dots[:, 3:4], ab_b[:, :], ALU.add))
            dve.tensor_copy(wext[:, D:D + 1], dots[:, 0:1]).then_inc(s_weights, 1)
            dve.tensor_copy(wdst[:, :], dots[:, 1:2].to_broadcast([P, P])).then_inc(s_weights, 1)
            dve.wait_ge(s_w1t, 1)
            dve.tensor_tensor(wb_t[:, :], bank[6][:, 0:D], ident[:, :], ALU.add).then_inc(s_w1c, 1)

            def h_out(i, j, t, n, r):
                dve.wait_ge(s_h[j], i + 1)
                dve.wait_ge(s_htab[j], 16 * i)
                dve.tensor_tensor(h_sb[0:r, j, 0:n, 0:D], split(bank[2 + j][0:r, 0:n * D]),
                                  b0_b[0:r, :].unsqueeze(1).to_broadcast([r, n, D]), ALU.add).then_inc(s_hs[j], 1)
                dve.tensor_scalar(h_sb[0:r, j, 0:n, D], bank[6 + j][0:r, 0:n], dots[0:r, 2:3], None, ALU.add).then_inc(s_hs[j], 1)
            per_batch(dve, h_out)

            for j in range(2):
                dve.wait_ge(s_sd[j], NBATCH // 2 + 1 - j)
            dve.wait_ge(s_const, 8)
            npass = dve.value_load(passes_i[0:1, 0:1], min_val=1, max_val=MAXP)

            def windows(l, v, it):
                for h in range(2):
                    dve.wait_ge(idx[l][h], v * 32 + 32)
                dve.tensor_copy(dst_f[:, :, :], dst_i[:, :, :]).then_inc(dstf[l], 1)
                dve.wait_ge(dstf[l], v + 1)
                dve.tensor_tensor(rel[:, :, :], dst_f[:, :, :],
                                  base_f[:, bass.ds(it * U, U)].unsqueeze(2).to_broadcast([P, U, K]), ALU.subtract).then_inc(relw[l], 1)
                return [dve.value_load(base_i[0:1, bass.ds(it * U + u, 1)], min_val=0, max_val=N) for u in range(U)]

            def one_hot(into, u, op):
                return dve.tensor_tensor(into, iota_w[:, :].unsqueeze(1).to_broadcast([P, K, WIN]),
                                         rel[:, u, :].unsqueeze(2).to_broadcast([P, K, WIN]), op)

            def move_on(l, m):
                dve.tensor_scalar(base_f[:, :], base_f[:, :], float(WIN), float(N), ALU.add, ALU.min).then_inc(moved[l], 1)
                dve.wait_ge(moved[l], m + 1)
                dve.tensor_copy(base_i[:, :], base_f[:, :]).then_inc(moved[l], 1)
                dve.wait_ge(moved[l], m + 2)

            def scores(n, v, u, base):
                s = u % 2
                dve.wait_ge(relw[0], v + 1)
                one_hot(hot[:, s, :, :], u, ALU.not_equal).then_inc(hotw[0], 1)
                dve.wait_ge(hotw[0], n + 1)
                dve.wait_ge(gath[0][u], v * K * 16 + K * 16)
                dve.scalar_tensor_tensor(comb[:, s, :, :], hot[:, s, :, :], MASKED,
                                         rows[:, u, :, D:D + 1].to_broadcast([P, K, WIN]), ALU.mult, ALU.add).then_inc(s_comb, 1)
                dve.wait_ge(s_comb, n + 1)
                dve.tensor_tensor(zed[:, s, :, :], comb[:, s, :, :],
                                  md[:, 1, bass.ds(base, WIN)].unsqueeze(1).to_broadcast([P, K, WIN]), ALU.add).then_inc(s_zed, 1)
                dve.wait_ge(s_zed, n + 1)
                if u >= 2:
                    dve.wait_ge(s_prob, n - 1)
                dve.scalar_tensor_tensor(lrel[:, s, 0:K, :], zed[:, s, :, :], LEAK, zed[:, s, :, :], ALU.mult, ALU.max).then_inc(s_leak, 1)

            def highest(n, u):
                dve.wait_ge(s_turn, n + 1)
                dve.reduce_max(top[:, u % 2:u % 2 + 1], bank[u % 2][0:WIN, :], AX).then_inc(s_top, 1)

            def below_max(n, u, base):
                s = u % 2
                running = md[:, 0, bass.ds(base, WIN)]
                dve.wait_ge(s_new, n)
                dve.tensor_copy(lrel[:, s, K, :], running).then_inc(s_old, 1)
                dve.wait_ge(s_old, n + 1)
                dve.wait_ge(s_max, n + 1)
                dve.tensor_tensor(running, running, bank[2 + s][:, 0:WIN], ALU.max).then_inc(s_new, 1)
                dve.wait_ge(s_new, n + 1)
                dve.tensor_tensor(lrel[:, s, :, :], lrel[:, s, :, :],
                                  running.unsqueeze(1).to_broadcast([P, K + 1, WIN]), ALU.subtract).then_inc(s_arg, 1)

            def add_up(l, n, v, u, into, base):
                s = u % 2
                running = into[:, :, bass.ds(base, WIN)]
                dve.wait_ge(acc[l], n)
                dve.wait_ge(sums[l][u], v + 1)
                if l == 0:
                    dve.tensor_tensor(running, running, prob[:, s, K:K + 1, :].to_broadcast([P, 2, WIN]), ALU.mult).then_inc(s_scaled, 1)
                    dve.wait_ge(s_scaled, n + 1)
                dve.tensor_tensor(running, running, bank[4 + s][:, 0:2 * WIN].rearrange("p (a c) -> p a c", a=2), ALU.add).then_inc(acc[l], 1)

            with dve.Fori(0, npass) as w:
                with dve.Fori(0, NB) as it:
                    n0, v = w * NG + it * U, w * NB + it
                    base = windows(0, v, it)
                    for u in range(U + 2):
                        if 1 <= u <= U:
                            highest(n0 + u - 1, u - 1)
                        if u < U:
                            scores(n0 + u, v, u, base[u])
                        if 1 <= u <= U:
                            below_max(n0 + u - 1, u - 1, base[u - 1])
                        if u >= 2:
                            add_up(0, n0 + u - 2, v, u - 2, agg, base[u - 2])
                move_on(0, w * 2)

            def means(l, F, i, j, t, n, r, buf, least):
                c = (n - 1) * P + r
                dve.wait_ge(F.mm[j], i)
                dve.wait_ge(acc[l], npass * NG)
                dve.tensor_scalar_max(inv[:, j, 0:c], buf[:, 1, cols(t, n, r)], least).then_inc(F.stats[j], 1)
                dve.wait_ge(F.stats[j], 3 * i + 1)
                dve.reciprocal(inv[:, j, 0:c], inv[:, j, 0:c]).then_inc(F.stats[j], 1)
                dve.wait_ge(F.stats[j], 3 * i + 2)
                dve.tensor_tensor(norm[:, j, 0:c], buf[:, 0, cols(t, n, r)], inv[:, j, 0:c], ALU.mult).then_inc(F.mean[j], 1)

            def residual(F, i, j, t, n, r):
                dve.wait_ge(F.mm[j], i + 1)
                dve.wait_ge(F.normed[j], i)
                dve.tensor_tensor(y_sb[0:r, j, 0, :] if n == 1 else y_sb[:, j, :, :], tiles(x_sb, t, n, r),
                                  bank[j][0:r, 0:D] if n == 1 else split(bank[j][:, :]), ALU.add).then_inc(F.y[j], 1)
                dve.wait_ge(F.y[j], i + 1)
                for m in range(n):
                    last = dve.bn_stats(stats[0:r, j, m, :], y_sb[0:r, j, m, :])
                last.then_inc(F.stats[j], 1)
                hold(dve, F.stats[j], 3 * i + 3)
                for m in range(n):
                    last = dve.bn_aggr(mv[0:r, j, m, :], stats[0:r, j, m, :])
                last.then_inc(F.mv[j], 1)

            def scales(F, i, j, n, r):
                dve.wait_ge(F.std[j], i + 1)
                dve.reciprocal(rstd[0:r, j, 0:n], std[0:r, j, 0:n]).then_inc(F.rstd[j], 1)
                dve.wait_ge(F.rstd[j], i + 1)
                dve.scalar_tensor_tensor(shift[0:r, j, 0:n], mv[0:r, j, 0:n, 0], -1.0, rstd[0:r, j, 0:n],
                                         ALU.mult, ALU.mult).then_inc(F.shift[j], 1)

            def end_first(i, j, t, n, r):
                means(0, F0, i, j, t, n, r, agg, TINY)
                residual(F0, i, j, t, n, r)
                scales(F0, i, j, n, r)
            dve.wait_ge(s_xload, 32)
            per_batch(dve, end_first)

            dve.tensor_copy(base_f[:, :], lohi[:, 0, :]).then_inc(moved[1], 1)
            dve.tensor_copy(base_i[:, :], lohi[:, 0, :]).then_inc(moved[1], 1)
            dve.wait_ge(moved[1], 2)
            dve.wait_ge(s_clear, 1)

            with dve.Fori(0, npass) as w:
                with dve.Fori(0, NB) as it:
                    n0, v = w * NG + it * U, w * NB + it
                    base = windows(1, v, it)
                    for u in range(U + 1):
                        if u < U:
                            dve.wait_ge(relw[1], v + 1)
                            one_hot(prob[:, u % 2, 0:K, :], u, ALU.is_equal).then_inc(hotw[1], 1)
                            dve.wait_ge(gath[1][u], v * K * 16 + K * 16)
                            dve.wait_ge(s_ef[u], v * 16 + 16)
                            dve.tensor_tensor(rows[:, u, :, 0:D], rows[:, u, :, 0:D], ef[:, u, :, :], ALU.add).then_inc(s_msg[u], 1)
                        if u >= 1:
                            add_up(1, n0 + u - 1, v, u - 1, md, base[u - 1])
                move_on(1, w * 2 + 2)

            for j in range(2):
                dve.wait_ge(s_owned[j], NBATCH // 2 + 1 - j)

            def end_second(i, j, t, n, r):
                means(1, F1, i, j, t, n, r, md, 1.0)
                residual(F1, i, j, t, n, r)
                scales(F1, i, j, n, r)
            per_batch(dve, end_second)


_INS = ['x', 'src', 'dst', 'edge_attr_128', 'L0_gnn_W', 'L0_gnn_b', 'L0_gnn_attn_w', 'L0_gnn_attn_b',
        'L0_gnn_mask_weights', 'L1_gnn_W', 'L1_gnn_b']
_OUTS = [((N, D), 'float32')]


def kernel(**inputs):
    import numpy as _np
    import concourse.bacc as _bacc
    from concourse import mybir as _mybir
    from concourse.bass_utils import run_bass_kernel_spmd as _run

    nc = _bacc.Bacc("TRN2", target_bir_lowering=False, num_devices=1)
    arrays, args = {}, []
    for name in _INS:
        a = _np.ascontiguousarray(inputs[name])
        arrays[f"in_{name}_dram"] = a
        args.append(nc.dram_tensor(f"in_{name}_dram", a.shape, _mybir.dt.from_np(a.dtype), kind="ExternalInput").ap())
    for i, (shape, dtype) in enumerate(_OUTS):
        dt = _mybir.dt.from_np(_np.dtype(dtype))
        args.append(nc.dram_tensor(f"out_{i}_dram", shape, dt, kind="ExternalOutput").ap())
    gnn_program(nc, *args)
    r = _run(nc, [arrays], core_ids=[0])
    got = tuple(r.results[0][f"out_{i}_dram"] for i in range(len(_OUTS)))
    return got[0]
```

```python
import concourse.bass as bass
from concourse import mybir
from contextlib import ExitStack

N = 6250
E = 106250
D = 128
P = 128
LEAK = 0.01
EPS = 1e-5

K = 4
GE = K * P
NG = -(-E // GE)
HOLE = NG * GE - E
U = 8
NB = NG // U
WIN = 40
MAXP = -(-N // WIN)
T = -(-N // P)
LAST = N - (T - 1) * P
Q = 4
COLS = N + WIN
NBATCH = (T - 1) // Q
XCUTS = 3
MASKED = -1.0e30
FLOOR = -1.0e25
TINY = 1.0e-30
assert NG % U == 0 and NBATCH % 2 == 0 and (T - 1) % Q == 0 and HOLE < GE


def gnn_program(nc, x, src, dst, edge, w0, b0, aw, ab, mask, w1, b1, out):
    fp32 = mybir.dt.float32
    i32 = mybir.dt.int32
    ALU = mybir.AluOpType
    ACT = mybir.ActivationFunctionType
    AX = mybir.AxisListType.X

    ctx = ExitStack()
    with ctx:
        def sb(name, shape, dt=fp32):
            return ctx.enter_context(nc.sbuf_tensor(name, shape, dt))

        def sem(name):
            return ctx.enter_context(nc.semaphore(name))

        htab = nc.dram_tensor("htab", [N, D + 1], fp32).ap()
        sdrow = nc.dram_tensor("sdrow", [T * P], fp32).ap()
        x1tab = nc.dram_tensor("x1tab", [N, D], fp32).ap()
        srcp = nc.dram_tensor("srcp", [NG * GE], i32).ap()
        dstp = nc.dram_tensor("dstp", [NG * GE], i32).ap()

        ident = sb("ident", [P, P])
        ones = sb("ones", [P, P])
        iota_i = sb("iota_i", [P, WIN], i32)
        iota_w = sb("iota_w", [P, WIN])
        steps_i = sb("steps_i", [P, MAXP], i32)
        steps = sb("steps", [P, MAXP])
        fill_i = sb("fill_i", [1, 2, HOLE], i32)
        w0_sb = sb("w0_sb", [P, D])
        wext = sb("wext", [P, D + 2])
        a_b = sb("a_b", [P, 2, D])
        bext = sb("bext", [P, D + 2])
        b1_b = sb("b1_b", [P, D])
        ab_b = sb("ab_b", [P, 1])
        mask_sb = sb("mask_sb", [P, 1])
        sig = sb("sig", [P, 3])
        prod = sb("prod", [P, 4, D])
        dots = sb("dots", [P, 4])
        w1_sb = sb("w1_sb", [P, 2 * D])
        wa_t = sb("wa_t", [P, D])
        wb_t = sb("wb_t", [P, D])
        eps_c = sb("eps_c", [P, 1])

        rng = sb("rng", [P, 2, GE], i32)
        ext = sb("ext", [P, 2, 2])
        lohi = sb("lohi", [P, 2, NG])
        span = sb("span", [P, NG])
        span_max = sb("span_max", [P, 1])
        reach = sb("reach", [P, MAXP])
        passes = sb("passes", [P, 1])
        passes_i = sb("passes_i", [P, 1], i32)
        base_f = sb("base_f", [P, NG])
        base_i = sb("base_i", [P, NG], i32)

        x_sb = sb("x_sb", [P, T, D])
        x_t = sb("x_t", [P, 2, Q * P])
        h_sb = sb("h_sb", [P, 2, Q, D + 2])
        sd_col = sb("sd_col", [P, T])
        sd_t = sb("sd_t", [T, P])
        o_sb = sb("o_sb", [P, 2, Q, D])
        stats = sb("stats", [P, 2, Q, 6])
        mv = sb("mv", [P, 2, Q, 2])
        std = sb("std", [P, 2, Q])
        rstd = sb("rstd", [P, 2, Q])
        shift = sb("shift", [P, 2, Q])
        weight = sb("weight", [P, 2, Q])
        inv = sb("inv", [P, 2, Q])
        md = sb("md", [P, 2, COLS])
        agg = sb("agg", [P, 2, COLS])

        src_i = sb("src_i", [P, U, K], i32)
        dst_i = sb("dst_i", [P, U, K], i32)
        dst_f = sb("dst_f", [P, U, K])
        rel = sb("rel", [P, U, K])
        rows = sb("rows", [P, U, K, D + 1])
        ef = sb("ef", [P, U, K, D])
        hot = sb("hot", [P, 2, K, WIN])
        comb = sb("comb", [P, 2, K, WIN])
        zed = sb("zed", [P, 2, K, WIN])
        lrel = sb("lrel", [P, 2, K + 1, WIN])
        prob = sb("prob", [P, 2, K + 1, WIN])
        wsum = sb("wsum", [P, 2, WIN])
        top = sb("top", [WIN, 2])

        bank = [ctx.enter_context(nc.psum_tensor(f"bank{i}", [P, 512], fp32)) for i in range(8)]

        def sems(name, n):
            return [sem(f"{name}{i}") for i in range(n)]

        s_const = sem("s_const")
        s_zero = sem("s_zero")
        s_fill = sem("s_fill")
        s_wload = sem("s_wload")
        s_x = sems("s_x", XCUTS)
        s_rng = sem("s_rng")
        s_padded = sem("s_padded")
        s_prep = sem("s_prep")
        s_gate = sem("s_gate")
        s_ext = sem("s_ext")
        s_lohi = sem("s_lohi")
        s_bases = sem("s_bases")
        s_weights = sem("s_weights")
        s_w1t = sem("s_w1t")
        s_w1c = sem("s_w1c")
        s_xt = sems("s_xt", 2)
        s_xtc = sems("s_xtc", 2)
        s_h = sems("s_h", 2)
        s_hs = sems("s_hs", 2)
        s_sdc = sem("s_sdc")
        s_sdt = sem("s_sdt")
        s_sds = sem("s_sds")
        s_sdd = sem("s_sdd")
        s_sd = sem("s_sd")
        s_htab = sems("s_htab", 2)
        s_clear = sem("s_clear")
        s_ot = sems("s_ot", 2)
        s_otc = sems("s_otc", 2)
        s_own = sems("s_own", 2)
        s_owned = sems("s_owned", 2)

        s_idx = sems("s_idx", 2)
        s_gath = sems("s_gath", U)
        s_dstf = sem("s_dstf")
        s_rel = sem("s_rel")
        s_hot = sem("s_hot")
        s_wsum = sem("s_wsum")
        s_sum = sems("s_sum", U)
        s_acc = sem("s_acc")
        s_moved = sem("s_moved")
        s_ef = sems("s_ef", U)
        s_msg = sems("s_msg", U)
        s_comb = sem("s_comb")
        s_zed = sem("s_zed")
        s_leak = sem("s_leak")
        s_turn = sem("s_turn")
        s_top = sem("s_top")
        s_max = sem("s_max")
        s_old = sem("s_old")
        s_new = sem("s_new")
        s_arg = sem("s_arg")
        s_prob = sem("s_prob")
        s_scaled = sem("s_scaled")

        class Finish:
            def __init__(self, l):
                self.weight = sems(f"{l}_weight", 2)
                self.first = sem(f"{l}_first")
                self.mm = sems(f"{l}_mm", 2)
                self.y = sems(f"{l}_y", 2)
                self.stats = sems(f"{l}_stats", 2)
                self.mv = sems(f"{l}_mv", 2)
                self.std = sems(f"{l}_std", 2)
                self.rstd = sems(f"{l}_rstd", 2)
                self.shift = sems(f"{l}_shift", 2)
                self.normed = sems(f"{l}_normed", 2)
                self.store = sems(f"{l}_store", 2)
                self.all_stored = [16 * (NBATCH // 2 + 1), 16 * (NBATCH // 2)]

        F0, F1 = Finish("f0"), Finish("f1")
        s_held = sem("s_held")

        def hold(eng, sem, value):
            eng.wait_ge(sem, value)
            eng.sem_inc(s_held, 1)

        block = ctx.enter_context(nc.Block())

        def per_batch(eng, body):
            with eng.Fori(0, NBATCH // 2) as i:
                for j in range(2):
                    body(i, j, (i * 2 + j) * Q, Q, P)
            body(NBATCH // 2, 0, T - 1, 1, LAST)

        def each_batch(body):
            for b in range(NBATCH + 1):
                n = Q if b < NBATCH else 1
                body(b // 2, b % 2, b * Q, n, P if b < NBATCH else LAST)

        def wait(eng, sem, value):
            if not (type(value) is int and value <= 0):
                eng.wait_ge(sem, value)

        def tile_rows(dram, t, n, r):
            if n == 1:
                return dram[t * P:t * P + r, :]
            return dram[bass.ds(t * P, n * P), :].rearrange("(t p) d -> p t d", p=P)

        def tiles(buf, t, n, r):
            return buf[0:r, t, :] if n == 1 else buf[:, bass.ds(t, n), :]

        def cols(t, n, r):
            return slice(t * P, t * P + r) if n == 1 else bass.ds(t * P, n * P)

        def split(ap):
            return ap.rearrange("p (t d) -> p t d", d=D)

        opening = [(u, u - 1 if u >= 1 else None, u - 2 if u >= 2 else None) for u in range(U)]
        middle = [(u, (u - 1) % U, (u - 2) % U) for u in range(U)]
        closing = [(U, U - 1, U - 2), (U + 1, None, U - 1)]

        @block.sync
        def _(sp):
            for into, what in ((mask_sb[:, :], mask.rearrange("(p a) -> p a", a=1)),
                               (w0_sb[:, :], w0), (w1_sb[:, :], w1),
                               (a_b[:, 0, :], aw[0:D, :].rearrange("d a -> a d").to_broadcast([P, D])),
                               (a_b[:, 1, :], aw[D:2 * D, :].rearrange("d a -> a d").to_broadcast([P, D])),
                               (bext[:, 0:D], b0.rearrange("(a d) -> a d", a=1).to_broadcast([P, D])),
                               (ab_b[:, :], ab.rearrange("(a d) -> a d", a=1).to_broadcast([P, 1])),
                               (b1_b[:, :], b1.rearrange("(a d) -> a d", a=1).to_broadcast([P, D]))):
                sp.dma_start(into, what).then_inc(s_wload, 16)
            half = NG - P
            sp.dma_start(rng[:, 0, :], dst[0:P * GE].rearrange("(g e) -> g e", g=P)).then_inc(s_rng, 16)
            sp.dma_start(rng[0:half - 1, 1, :], dst[P * GE:(NG - 1) * GE].rearrange("(g e) -> g e", g=half - 1)).then_inc(s_rng, 16)
            sp.dma_start(rng[half - 1:half, 1, :], dst[E - GE:E].rearrange("(g e) -> g e", g=1)).then_inc(s_rng, 16)
            full = (NG - 1) * GE
            sp.wait_ge(s_fill, 2)
            for m, (lst, pad) in enumerate(((src, srcp), (dst, dstp))):
                sp.dma_start(pad[0:full].rearrange("(a b) -> a b", b=GE), lst[0:full].rearrange("(a b) -> a b", b=GE)).then_inc(s_padded, 16)
                sp.dma_start(pad[full:full + HOLE].rearrange("(a b) -> a b", a=1), fill_i[:, m, :]).then_inc(s_padded, 16)
                sp.dma_start(pad[full + HOLE:NG * GE].rearrange("(a b) -> a b", a=1), lst[full:E].rearrange("(a b) -> a b", a=1)).then_inc(s_padded, 16)
            sp.wait_ge(s_padded, 96)

            def store_h(i, j, t, n, r):
                sp.wait_ge(s_hs[j], 2 * i + 2)
                sp.dma_start(tile_rows(htab, t, n, r), h_sb[0:r, j, 0, 0:D + 1] if n == 1 else h_sb[:, j, :, 0:D + 1]).then_inc(s_htab[j], 16)
            per_batch(sp, store_h)

            sp.wait_ge(s_bases, 1)
            npass = sp.value_load(passes_i[0:1, 0:1], min_val=1, max_val=MAXP)

            def load_body(l, v, v1, it, last):
                H = U // 2
                for h in range(2):
                    sp.wait_ge(s_dstf, v)
                    for u in range(h * H, (h + 1) * H):
                        sp.wait_ge(s_gath[u], v * K * 16)
                    for buf, lst in ((src_i, srcp), (dst_i, dstp)):
                        sp.dma_start(buf[:, h * H:(h + 1) * H, :],
                                     lst[bass.ds((it * U + h * H) * GE, H * GE)].rearrange("(g p k) -> p g k", p=P, k=K)).then_inc(s_idx[h], 16)
                    for u in range(h * H, (h + 1) * H) if l else ():
                        e0 = E - GE if last and u == U - 1 else (it * U + u) * GE
                        sp.wait_ge(s_msg[u], v1)
                        sp.dma_start(ef[:, u, :, :], edge[bass.ds(e0, GE), :].rearrange("(p k) d -> p k d", k=K)).then_inc(s_ef[u], 16)

            def load_edges(l):
                with sp.Fori(0, npass) as w:
                    v = (w + l * npass) * NB
                    with sp.Fori(0, NB - 1) as it:
                        load_body(l, v + it, w * NB + it, it, False)
                    load_body(l, v + NB - 1, w * NB + NB - 1, NB - 1, True)

            load_edges(0)

            def store_x1(i, j, t, n, r):
                sp.wait_ge(F0.normed[j], i + 1)
                sp.dma_start(tile_rows(x1tab, t, n, r), tiles(x_sb, t, n, r)).then_inc(F0.store[j], 16)
            per_batch(sp, store_x1)
            load_edges(1)

            def store_out(i, j, t, n, r):
                sp.wait_ge(F1.normed[j], i + 1)
                sp.dma_start(tile_rows(out, t, n, r), o_sb[0:r, j, 0, :] if n == 1 else o_sb[:, j, :, :]).then_inc(F1.store[j], 16)
            per_batch(sp, store_out)
            for j in range(2):
                sp.wait_ge(F1.store[j], F1.all_stored[j])

        @block.gpsimd
        def _(pool):
            pool.memset(fill_i[:, 0, :], 0).then_inc(s_fill, 1)
            pool.memset(fill_i[:, 1, :], -1).then_inc(s_fill, 1)
            pool.memset(ident[:, :], 0.0).then_inc(s_zero, 1)
            pool.wait_ge(s_zero, 1)
            pool.affine_select(out=ident[:, :], in_=ident[:, :], compare_op=ALU.not_equal, fill=1.0, base=0,
                               pattern=[[-1, P]], channel_multiplier=1).then_inc(s_const, 1)
            pool.memset(ones[:, :], 1.0).then_inc(s_const, 1)
            pool.memset(sd_col[:, :], 0.0).then_inc(s_const, 1)
            pool.iota(iota_i[:, :], pattern=[[1, WIN]], base=0, channel_multiplier=0).then_inc(s_const, 1)
            pool.iota(steps_i[:, :], pattern=[[WIN, MAXP]], base=0, channel_multiplier=0).then_inc(s_const, 1)
            pool.memset(eps_c[:, :], EPS).then_inc(s_const, 1)
            pool.memset(md[:, 1, N:COLS], 0.0).then_inc(s_const, 1)
            pool.memset(md[:, 0, :], FLOOR).then_inc(s_const, 1)
            pool.memset(agg[:, :, :], 0.0).then_inc(s_const, 1)
            pool.wait_ge(s_bases, 1)
            npass = pool.value_load(passes_i[0:1, 0:1], min_val=1, max_val=MAXP)

            def gather_rows(l, table, width):
                with pool.Fori(0, npass) as w:
                    with pool.Fori(0, NB) as it:
                        v = (w + l * npass) * NB + it
                        for u in range(U):
                            if u % (U // 2) == 0:
                                pool.wait_ge(s_idx[u // (U // 2)], v * 32 + 32)
                            hold(pool, s_sum[u], v)
                            for k in range(K):
                                pool.indirect_dma_start(
                                    rows[:, u, k, 0:width], None, table[:, :],
                                    bass.IndirectOffsetOnAxis(src_i[:, u, k:k + 1], 0)).then_inc(s_gath[u], 16)

            for j in range(2):
                pool.wait_ge(s_htab[j], F0.all_stored[j])
            gather_rows(0, htab, D + 1)
            pool.wait_ge(F0.first, 1)
            pool.memset(md[:, :, :], 0.0).then_inc(s_clear, 1)
            for j in range(2):
                pool.wait_ge(F0.store[j], F0.all_stored[j])
            gather_rows(1, x1tab, D)

        @block.tensor
        def _(pe):
            pe.wait_ge(s_const, 2)
            pe.wait_ge(s_wload, 128)
            for m in range(2):
                last = pe.transpose(bank[6 + m][:, 0:D], w1_sb[:, m * D:(m + 1) * D], ident[:, :])
            last.then_inc(s_w1t, 1)
            pe.wait_ge(s_w1c, 2)
            pe.wait_ge(s_weights, 1)

            def turn_x(b):
                i, j, n, r = b // 2, b % 2, Q if b < NBATCH else 1, P if b < NBATCH else LAST
                c = min(b * XCUTS // NBATCH, XCUTS - 1)
                pe.wait_ge(s_x[c], 32 if c == XCUTS - 1 else 16)
                wait(pe, s_xtc[j], i)
                for m in range(n):
                    last = pe.transpose(bank[j][:, m * P:m * P + r], x_sb[0:r, b * Q + m, :], ident[0:r, 0:r])
                last.then_inc(s_xt[j], 1)

            def node_scores(i, j, t, n, r):
                if i * 2 + j < NBATCH:
                    turn_x(i * 2 + j + 1)
                pe.wait_ge(s_xtc[j], i + 1)
                wait(pe, s_hs[j], 2 * i)
                for m in range(n):
                    at = m % 2 * (D + 2)
                    last = pe.matmul(bank[2 + 2 * j + m // 2][0:r, at:at + D + 2], x_t[:, j, m * P:m * P + r], wext[:, :], start=True, stop=True)
                last.then_inc(s_h[j], 1)
            turn_x(0)
            pe.wait_ge(s_ext, 4)
            for m in range(2):
                for c, n in ((0, P), (1, NG - P)):
                    last = pe.matmul(bank[5][:, m * NG + c * P:m * NG + c * P + n],
                                     ext[0:n, c, m:m + 1].to_broadcast([n, P]), ident[0:n, 0:n], start=True, stop=True)
            last.then_inc(s_lohi, 1)
            pe.wait_ge(s_bases, 1)
            each_batch(node_scores)
            pe.wait_ge(s_sdc, 1)
            pe.transpose(bank[6][0:T, 0:P], sd_col[:, :], ident[:, :]).then_inc(s_sdt, 1)
            pe.wait_ge(s_bases, 1)
            npass = pe.value_load(passes_i[0:1, 0:1], min_val=1, max_val=MAXP)

            def weighted(u):
                for k in range(K):
                    last = pe.matmul(bank[4 + u % 2][:, 0:WIN], rows[:, u, k, 0:D], prob[:, u % 2, k, :],
                                     start=(k == 0), stop=(k == K - 1))
                return last

            def weights(u):
                return pe.matmul(bank[4 + u % 2][:, WIN:2 * WIN], ones[:, :], wsum[:, u % 2, :], start=True, stop=True)

            def steps_first(n0, us):
                for u, old, older in us:
                    if old is not None:
                        pe.wait_ge(s_top, n0 + u)
                        pe.matmul(bank[2 + old % 2][:, 0:WIN], top[:, old % 2:old % 2 + 1].to_broadcast([WIN, P]),
                                  ident[0:WIN, 0:WIN], start=True, stop=True).then_inc(s_max, 1)
                    if older is not None:
                        pe.wait_ge(s_wsum, n0 + u - 1)
                        weights(older).then_inc(s_sum[older], 1)
                    if u < U:
                        hold(pe, s_leak, n0 + u + 1)
                        for k in range(K):
                            last = pe.transpose(bank[u % 2][0:WIN, k * P:(k + 1) * P], lrel[:, u % 2, k, :], ident[:, :])
                        last.then_inc(s_turn, 1)
                    if old is not None:
                        pe.wait_ge(s_prob, n0 + u)
                        weighted(old)

            with pe.Fori(0, npass) as w:
                steps_first(w * NG, opening)
                with pe.Fori(1, NB) as it:
                    steps_first(w * NG + it * U, middle)
                steps_first(w * NG + (NB - 1) * U, closing)

            def turn_back(i, j, t, n, r):
                pe.wait_ge(F0.first, 1)
                wait(pe, F0.y[j], i)
                for m in range(n):
                    c = slice((t + m) * P, (t + m) * P + r)
                    pe.transpose(bank[2 + j][0:r, m * D:(m + 1) * D], agg[:, 1, c], ident[:, :])
                    last = pe.transpose(bank[j][0:r, m * D:(m + 1) * D], agg[:, 0, c], ident[:, :])
                last.then_inc(F0.mm[j], 1)
            each_batch(turn_back)

            def turn_x1(b):
                i, j, n, r = b // 2, b % 2, Q if b < NBATCH else 1, P if b < NBATCH else LAST
                pe.wait_ge(F0.normed[j], i + 1)
                wait(pe, s_otc[j], i)
                for m in range(n):
                    last = pe.transpose(bank[4 + j][:, m * P:m * P + r], x_sb[0:r, b * Q + m, :], ident[0:r, 0:r])
                last.then_inc(s_ot[j], 1)

            def own_part(i, j, t, n, r):
                if i * 2 + j < NBATCH:
                    turn_x1(i * 2 + j + 1)
                pe.wait_ge(s_otc[j], i + 1)
                wait(pe, s_owned[j], i)
                for m in range(n):
                    last = pe.matmul(bank[6 + j][0:r, m * D:(m + 1) * D], x_t[:, j, m * P:m * P + r], wb_t[:, :], start=True, stop=True)
                last.then_inc(s_own[j], 1)
            turn_x1(0)
            each_batch(own_part)

            with pe.Fori(0, npass) as w:
                with pe.Fori(0, NB) as it:
                    for u in range(U):
                        pe.wait_ge(s_msg[u], w * NB + it + 1)
                        weighted(u)
                        pe.wait_ge(s_wsum, (w + npass) * NG + it * U + u + 1)
                        weights(u).then_inc(s_sum[u], 1)

            def neighbours(i, j, t, n, r):
                pe.wait_ge(F1.first, 1)
                wait(pe, F1.y[j], i)
                for m in range(n):
                    c = slice((t + m) * P, (t + m) * P + r)
                    pe.transpose(bank[2 + j][0:r, m * D:(m + 1) * D], md[:, 1, c], ident[:, :])
                    last = pe.matmul(bank[j][0:r, m * D:(m + 1) * D], md[:, 0, c], wa_t[:, :], start=True, stop=True)
                last.then_inc(F1.mm[j], 1)
            each_batch(neighbours)

        @block.scalar
        def _(act):
            act.wait_ge(s_wload, 128)
            act.activation(sig[:, 0:1], mask_sb[:, :], ACT.Exp, scale=-1.0).then_inc(s_gate, 1)
            for c in range(XCUTS):
                lo, hi = (T - 1) * c // XCUTS, (T - 1) * (c + 1) // XCUTS
                act.dma_start(x_sb[:, lo:hi, :], x[lo * P:hi * P, :].rearrange("(t p) d -> p t d", p=P)).then_inc(s_x[c], 16)
            act.dma_start(x_sb[0:LAST, T - 1, :], x[(T - 1) * P:N, :]).then_inc(s_x[XCUTS - 1], 16)
            act.wait_ge(s_w1t, 1)
            act.activation(wa_t[:, :], bank[6][:, 0:D], ACT.Copy).then_inc(s_w1c, 1)

            def x_out(i, j, t, n, r):
                c = (n - 1) * P + r
                act.wait_ge(s_xt[j], i + 1)
                act.wait_ge(s_h[j], i)
                act.activation(x_t[:, j, 0:c], bank[j][:, 0:c], ACT.Copy).then_inc(s_xtc[j], 1)
            per_batch(act, x_out)
            act.wait_ge(s_sdt, 1)
            act.activation(sd_t[:, :], bank[6][0:T, 0:P], ACT.Copy).then_inc(s_sds, 1)
            act.wait_ge(s_sds, 1)
            act.dma_start(sdrow.rearrange("(t p) -> t p", p=P), sd_t[:, :]).then_inc(s_sdd, 16)
            act.wait_ge(s_sdd, 16)
            act.dma_start(md[:, 1, 0:N], sdrow[0:N].rearrange("(a n) -> a n", a=1).to_broadcast([P, N])).then_inc(s_sd, 16)

            act.wait_ge(s_bases, 1)
            npass = act.value_load(passes_i[0:1, 0:1], min_val=1, max_val=MAXP)
            with act.Fori(0, npass) as w:
                with act.Fori(0, NB) as it:
                    for u in range(U):
                        act.wait_ge(s_arg, w * NG + it * U + u + 1)
                        act.activation(prob[:, u % 2, :, :], lrel[:, u % 2, :, :], ACT.Exp).then_inc(s_prob, 1)

            def norm_rows(F, i, j, t, n, r, into):
                act.wait_ge(F.mv[j], i + 1)
                act.activation(std[0:r, j, 0:n], mv[0:r, j, 0:n, 1], ACT.Sqrt, bias=eps_c[0:r, :]).then_inc(F.std[j], 1)
                act.wait_ge(F.shift[j], i + 1)
                for m in range(n):
                    last = act.activation(into(m), tiles(x_sb, t + m, 1, r), ACT.Identity,
                                          bias=shift[0:r, j, m:m + 1], scale=rstd[0:r, j, m:m + 1])
                last.then_inc(F.normed[j], 1)
            per_batch(act, lambda i, j, t, n, r: norm_rows(F0, i, j, t, n, r, lambda m: tiles(x_sb, t + m, 1, r)))

            def own_copy(i, j, t, n, r):
                c = (n - 1) * P + r
                act.wait_ge(s_ot[j], i + 1)
                act.wait_ge(s_own[j], i)
                act.activation(x_t[:, j, 0:c], bank[4 + j][:, 0:c], ACT.Copy).then_inc(s_otc[j], 1)
            per_batch(act, own_copy)

            def norm_out(i, j, t, n, r):
                act.wait_ge(F1.store[j], 16 * i)
                norm_rows(F1, i, j, t, n, r, lambda m: o_sb[0:r, j, m, :])
            per_batch(act, norm_out)

        @block.vector
        def _(dve):
            step = [0]

            def then(ins):
                step[0] += 1
                ins.then_inc(s_prep, 1)
                dve.wait_ge(s_prep, step[0])

            dve.wait_ge(s_wload, 128)
            dve.wait_ge(s_gate, 1)
            then(dve.tensor_scalar_add(sig[:, 1:2], sig[:, 0:1], 1.0))
            then(dve.reciprocal(sig[:, 2:3], sig[:, 1:2]))
            then(dve.tensor_scalar(wext[:, 0:D], w0_sb[:, :], sig[:, 2:3], None, ALU.mult))
            for i in range(2):
                then(dve.tensor_tensor(prod[:, i, :], wext[:, 0:D], a_b[:, i, :], ALU.mult))
                then(dve.tensor_tensor(prod[:, 2 + i, :], bext[:, 0:D], a_b[:, i, :], ALU.mult))
            then(dve.tensor_reduce(dots[:, :], prod[:, :, :], AX, ALU.add))
            then(dve.tensor_copy(bext[:, D:D + 1], dots[:, 2:3]))
            then(dve.tensor_tensor(bext[:, D + 1:D + 2], dots[:, 3:4], ab_b[:, :], ALU.add))
            dve.tensor_copy(wext[:, D:D + 2], dots[:, 0:2]).then_inc(s_weights, 1)
            dve.wait_ge(s_w1t, 1)
            dve.wait_ge(s_const, 1)
            dve.tensor_tensor(wb_t[:, :], bank[7][:, 0:D], ident[:, :], ALU.add).then_inc(s_w1c, 1)
            dve.wait_ge(s_rng, 48)
            for c, n in ((0, P), (1, NG - P)):
                dve.tensor_reduce(ext[0:n, c, 0:1], rng[0:n, c, :], AX, ALU.min).then_inc(s_ext, 1)
                dve.tensor_reduce(ext[0:n, c, 1:2], rng[0:n, c, :], AX, ALU.max).then_inc(s_ext, 1)
            dve.wait_ge(s_const, 5)
            then(dve.tensor_copy(iota_w[:, :], iota_i[:, :]))
            then(dve.tensor_copy(steps[:, :], steps_i[:, :]))
            dve.wait_ge(s_lohi, 1)
            then(dve.tensor_copy(lohi[:, :, :], bank[5][:, 0:2 * NG].rearrange("p (m g) -> p m g", m=2)))
            then(dve.tensor_tensor(span[:, :], lohi[:, 1, :], lohi[:, 0, :], ALU.subtract))
            then(dve.reduce_max(span_max[:, :], span[:, :], AX))
            then(dve.tensor_scalar(reach[:, :], steps[:, :], span_max[:, 0:1], None, ALU.is_le))
            then(dve.tensor_reduce(passes[:, :], reach[:, :], AX, ALU.add))
            then(dve.tensor_copy(passes_i[:, :], passes[:, :]))
            then(dve.tensor_copy(base_f[:, :], lohi[:, 0, :]))
            dve.tensor_copy(base_i[:, :], lohi[:, 0, :]).then_inc(s_bases, 1)

            def h_out(i, j, t, n, r):
                dve.wait_ge(s_h[j], i + 1)
                dve.wait_ge(s_htab[j], 16 * i)
                for m in range(0, n, 2):
                    q = min(2, n - m)
                    last = dve.tensor_tensor(h_sb[0:r, j, m:m + q, :],
                                             bank[2 + 2 * j + m // 2][0:r, 0:q * (D + 2)].rearrange("p (t d) -> p t d", t=q),
                                             bext[0:r, :].unsqueeze(1).to_broadcast([r, q, D + 2]), ALU.add)
                last.then_inc(s_hs[j], 1)
                dve.wait_ge(s_hs[j], 2 * i + 1)
                dve.tensor_copy(sd_col[0:r, bass.ds(t, n)], h_sb[0:r, j, 0:n, D + 1]).then_inc(s_hs[j], 1)
            per_batch(dve, h_out)
            dve.wait_ge(s_hs[0], 2 * (NBATCH // 2 + 1))
            dve.sem_inc(s_sdc, 1)
            dve.wait_ge(s_sd, 16)
            dve.wait_ge(s_const, 9)
            dve.wait_ge(s_bases, 1)
            npass = dve.value_load(passes_i[0:1, 0:1], min_val=1, max_val=MAXP)

            def windows(v, it):
                for h in range(2):
                    dve.wait_ge(s_idx[h], v * 32 + 32)
                dve.tensor_copy(dst_f[:, :, :], dst_i[:, :, :]).then_inc(s_dstf, 1)
                dve.wait_ge(s_dstf, v + 1)
                dve.tensor_tensor(rel[:, :, :], dst_f[:, :, :],
                                  base_f[:, bass.ds(it * U, U)].unsqueeze(2).to_broadcast([P, U, K]), ALU.subtract).then_inc(s_rel, 1)

            def bases(lo, n):
                _, found = nc.values_load_multi_w_load_instructions(
                    base_i[0:1, bass.ds(lo, n)], (mybir.EngineType.DVE,), min_val=0, max_val=N,
                    skip_runtime_bounds_check_because="they are clamped where they are made")
                return list(found)

            def one_hot(into, u, op):
                return dve.tensor_tensor(into, iota_w[:, :].unsqueeze(1).to_broadcast([P, K, WIN]),
                                         rel[:, u, :].unsqueeze(2).to_broadcast([P, K, WIN]), op)

            def move_on(m):
                dve.tensor_scalar(base_f[:, :], base_f[:, :], float(WIN), float(N), ALU.add, ALU.min).then_inc(s_moved, 1)
                dve.wait_ge(s_moved, m + 1)
                dve.tensor_copy(base_i[:, :], base_f[:, :]).then_inc(s_moved, 1)
                hold(dve, s_moved, m + 2)

            def add_weights(l, n, h):
                if l == 0:
                    dve.wait_ge(s_prob, n + 1)
                else:
                    dve.wait_ge(s_hot, n + 1)
                dve.tensor_reduce(wsum[:, h, :], prob[:, h, 0:K, :].rearrange("p k c -> p c k"), AX, ALU.add).then_inc(s_wsum, 1)

            def steps_first(n0, v, us, base):
                for u, old, older in us:
                    n, s = n0 + u, u % 2
                    now = u < U
                    if now:
                        dve.wait_ge(s_rel, v + 1)
                        one_hot(hot[:, s, :, :], u, ALU.not_equal).then_inc(s_hot, 1)
                    if old is not None:
                        o = old % 2
                        dve.wait_ge(s_turn, n)
                        dve.reduce_max(top[:, o:o + 1], bank[o][0:WIN, :], AX).then_inc(s_top, 1)
                    if now:
                        dve.wait_ge(s_hot, n + 1)
                        dve.wait_ge(s_gath[u], v * K * 16 + K * 16)
                        dve.scalar_tensor_tensor(comb[:, s, :, :], hot[:, s, :, :], MASKED,
                                                 rows[:, u, :, D:D + 1].to_broadcast([P, K, WIN]), ALU.mult, ALU.add).then_inc(s_comb, 1)
                    if older is not None:
                        add_weights(0, n - 2, older % 2)
                    if now:
                        dve.wait_ge(s_comb, n + 1)
                        dve.tensor_tensor(zed[:, s, :, :], comb[:, s, :, :],
                                          md[:, 1, bass.ds(base[u + 2], WIN)].unsqueeze(1).to_broadcast([P, K, WIN]), ALU.add).then_inc(s_zed, 1)
                    if old is not None:
                        running = md[:, 0, bass.ds(base[u + 1], WIN)]
                        dve.wait_ge(s_new, n - 1)
                        dve.tensor_copy(lrel[:, o, K, :], running).then_inc(s_old, 1)
                    if older is not None:
                        agg_run = agg[:, :, bass.ds(base[u], WIN)]
                        dve.wait_ge(s_acc, n - 2)
                        dve.tensor_tensor(agg_run, agg_run, prob[:, s, K:K + 1, :].to_broadcast([P, 2, WIN]), ALU.mult).then_inc(s_scaled, 1)
                    if now:
                        dve.wait_ge(s_zed, n + 1)
                        if older is not None:
                            dve.wait_ge(s_prob, n - 1)
                        dve.scalar_tensor_tensor(lrel[:, s, 0:K, :], zed[:, s, :, :], LEAK, zed[:, s, :, :], ALU.mult, ALU.max).then_inc(s_leak, 1)
                    if old is not None:
                        dve.wait_ge(s_old, n)
                        dve.wait_ge(s_max, n)
                        dve.tensor_tensor(running, running, bank[2 + o][:, 0:WIN], ALU.max).then_inc(s_new, 1)
                    if older is not None:
                        dve.wait_ge(s_scaled, n - 1)
                        dve.wait_ge(s_sum[older], v + 1 if u >= 2 else v)
                        dve.tensor_tensor(agg_run, agg_run, bank[4 + s][:, 0:2 * WIN].rearrange("p (a c) -> p a c", a=2), ALU.add).then_inc(s_acc, 1)
                    if old is not None:
                        dve.wait_ge(s_new, n)
                        dve.tensor_tensor(lrel[:, o, :, :], lrel[:, o, :, :],
                                          running.unsqueeze(1).to_broadcast([P, K + 1, WIN]), ALU.subtract).then_inc(s_arg, 1)

            with dve.Fori(0, npass) as w:
                windows(w * NB, 0)
                steps_first(w * NG, w * NB, opening, [None, None] + bases(0, U))
                with dve.Fori(1, NB) as it:
                    windows(w * NB + it, it)
                    steps_first(w * NG + it * U, w * NB + it, middle, bases(it * U - 2, U + 2))
                steps_first(w * NG + (NB - 1) * U, w * NB + NB - 1, closing, [None] * U + bases(NG - 2, 2) + [None, None])
                move_on(w * 2)
            dve.wait_ge(s_acc, npass * NG)
            dve.sem_inc(F0.first, 1)

            def residual(F, i, j, t, n, r, least):
                dve.wait_ge(F.mm[j], i + 1)
                dve.tensor_scalar_max(weight[0:r, j, 0:n], split(bank[2 + j][0:r, 0:n * D])[:, :, 0], least).then_inc(F.weight[j], 1)
                dve.wait_ge(F.weight[j], 2 * i + 1)
                dve.reciprocal(inv[0:r, j, 0:n], weight[0:r, j, 0:n]).then_inc(F.weight[j], 1)
                dve.wait_ge(F.weight[j], 2 * i + 2)
                for m in range(n):
                    last = dve.scalar_tensor_tensor(tiles(x_sb, t + m, 1, r), bank[j][0:r, m * D:(m + 1) * D], inv[0:r, j, m:m + 1],
                                                    tiles(x_sb, t + m, 1, r), ALU.mult, ALU.add)
                last.then_inc(F.y[j], 1)
                hold(dve, F.y[j], i + 1)
                for m in range(n):
                    last = dve.bn_stats(stats[0:r, j, m, :], tiles(x_sb, t + m, 1, r))
                last.then_inc(F.stats[j], 1)
                hold(dve, F.stats[j], i + 1)
                for m in range(n):
                    last = dve.bn_aggr(mv[0:r, j, m, :], stats[0:r, j, m, :])
                last.then_inc(F.mv[j], 1)

            def scales(F, i, j, n, r):
                dve.wait_ge(F.normed[j], i)
                dve.wait_ge(F.std[j], i + 1)
                dve.reciprocal(rstd[0:r, j, 0:n], std[0:r, j, 0:n]).then_inc(F.rstd[j], 1)
                dve.wait_ge(F.rstd[j], i + 1)
                dve.scalar_tensor_tensor(shift[0:r, j, 0:n], mv[0:r, j, 0:n, 0], -1.0, rstd[0:r, j, 0:n],
                                         ALU.mult, ALU.mult).then_inc(F.shift[j], 1)

            def end_layer(F, least):
                residual(F, 0, 0, 0, Q, P, least)
                with dve.Fori(0, NBATCH // 2 - 1) as i:
                    residual(F, i, 1, (i * 2 + 1) * Q, Q, P, least)
                    scales(F, i, 0, Q, P)
                    residual(F, i + 1, 0, (i * 2 + 2) * Q, Q, P, least)
                    scales(F, i, 1, Q, P)
                h = NBATCH // 2
                residual(F, h - 1, 1, (NBATCH - 1) * Q, Q, P, least)
                scales(F, h - 1, 0, Q, P)
                residual(F, h, 0, T - 1, 1, LAST, least)
                scales(F, h - 1, 1, Q, P)
                scales(F, h, 0, 1, LAST)
            end_layer(F0, TINY)

            def own_out(i, j, t, n, r):
                dve.wait_ge(s_own[j], i + 1)
                dve.tensor_tensor(tiles(x_sb, t, n, r), bank[6 + j][0:r, 0:D] if n == 1 else split(bank[6 + j][:, :]),
                                  b1_b[0:r, :] if n == 1 else b1_b[:, :].unsqueeze(1).to_broadcast([P, n, D]), ALU.add).then_inc(s_owned[j], 1)
            for j in range(2):
                dve.wait_ge(F0.store[j], F0.all_stored[j])
            per_batch(dve, own_out)

            dve.tensor_copy(base_f[:, :], lohi[:, 0, :]).then_inc(s_moved, 1)
            dve.tensor_copy(base_i[:, :], lohi[:, 0, :]).then_inc(s_moved, 1)
            hold(dve, s_moved, npass * 2 + 2)
            dve.wait_ge(s_clear, 1)

            def add_up(n, v, u, at):
                running = md[:, :, bass.ds(at, WIN)]
                dve.wait_ge(s_acc, n)
                dve.wait_ge(s_sum[u % U], v + 1 if u >= 0 else v)
                dve.tensor_tensor(running, running, bank[4 + u % 2][:, 0:2 * WIN].rearrange("p (a c) -> p a c", a=2), ALU.add).then_inc(s_acc, 1)

            def steps_second(n0, v, v1, us, base):
                for u, old, _ in us:
                    dve.wait_ge(s_rel, v + 1)
                    one_hot(prob[:, u % 2, 0:K, :], u, ALU.is_equal).then_inc(s_hot, 1)
                    dve.wait_ge(s_gath[u], v * K * 16 + K * 16)
                    dve.wait_ge(s_ef[u], v1 * 16 + 16)
                    dve.tensor_tensor(rows[:, u, :, 0:D], rows[:, u, :, 0:D], ef[:, u, :, :], ALU.add).then_inc(s_msg[u], 1)
                    add_weights(1, n0 + u, u % 2)
                    if old is not None:
                        add_up(n0 + u - 1, v, u - 1, base[u + 1])

            with dve.Fori(0, npass) as w:
                n0, v = (w + npass) * NG, (w + npass) * NB
                windows(v, 0)
                steps_second(n0, v, w * NB, opening, [None, None] + bases(0, U))
                with dve.Fori(1, NB) as it:
                    windows(v + it, it)
                    steps_second(n0 + it * U, v + it, w * NB + it, middle, bases(it * U - 2, U + 2))
                add_up(n0 + NG - 1, v + NB - 1, U - 1, bases(NG - 1, 1)[0])
                move_on((w + npass) * 2 + 2)
            dve.wait_ge(s_acc, npass * (2 * NG))
            dve.sem_inc(F1.first, 1)
            end_layer(F1, 1.0)


_INS = ['x', 'src', 'dst', 'edge_attr_128', 'L0_gnn_W', 'L0_gnn_b', 'L0_gnn_attn_w', 'L0_gnn_attn_b',
        'L0_gnn_mask_weights', 'L1_gnn_W', 'L1_gnn_b']
_OUTS = [((N, D), 'float32')]


def kernel(**inputs):
    import numpy as _np
    import concourse.bacc as _bacc
    from concourse import mybir as _mybir
    from concourse.bass_utils import run_bass_kernel_spmd as _run

    nc = _bacc.Bacc("TRN2", target_bir_lowering=False, num_devices=1)
    arrays, args = {}, []
    for name in _INS:
        a = _np.ascontiguousarray(inputs[name])
        arrays[f"in_{name}_dram"] = a
        args.append(nc.dram_tensor(f"in_{name}_dram", a.shape, _mybir.dt.from_np(a.dtype), kind="ExternalInput").ap())
    for i, (shape, dtype) in enumerate(_OUTS):
        dt = _mybir.dt.from_np(_np.dtype(dtype))
        args.append(nc.dram_tensor(f"out_{i}_dram", shape, dt, kind="ExternalOutput").ap())
    gnn_program(nc, *args)
    r = _run(nc, [arrays], core_ids=[0])
    got = tuple(r.results[0][f"out_{i}_dram"] for i in range(len(_OUTS)))
    return got[0]
```
